# Optimizing a Trainium2 kernel written in Bass

```python
import numpy as np
import jax
import jax.numpy as jnp

def _softmax(x, axis=-1):
    return jax.nn.softmax(x, axis=axis)

def _gelu(x):
    return jax.nn.gelu(x, approximate=True)

def _silu(x):
    return jax.nn.silu(x)

def _sigmoid(x):
    return jax.nn.sigmoid(x)

def _layernorm(x, axis=-1, eps=1e-05):
    m = jnp.mean(x, axis=axis, keepdims=True)
    v = jnp.var(x, axis=axis, keepdims=True)
    return (x - m) / jnp.sqrt(v + eps)

def _scatter_add(tgt, idx, src, axis=0):
    return tgt.at[idx].add(src)

def _segment_sum(src, seg, n):
    return jax.ops.segment_sum(src, seg, n)
kernel_name = 'mk_gnn_resnorm_d1_gnn_r32_f482c8'

def setup_inputs(seed: int=0):
    np.random.seed(seed)
    _w = jnp.asarray

    def _rec_inputs():
        import jax
        import jax.numpy as jnp
        _gk = jax.random.key(seed)
        x = -0.0001006 + 1 * jax.random.normal(jax.random.fold_in(_gk, 1), (50000, 96), jnp.float32)
        src = jax.random.randint(jax.random.fold_in(_gk, 2), (50000,), 0, 50000, jnp.int32)
        dst = jax.random.randint(jax.random.fold_in(_gk, 3), (50000,), 0, 50000, jnp.int32)
        _o = jnp.argsort(dst, stable=True)
        src = src[_o]
        dst = dst[_o]
        edge_attr_32 = 0.000196303 + 1.00016 * jax.random.normal(jax.random.fold_in(_gk, 11), (50000, 32), jnp.float32)
        return (x, src, dst, edge_attr_32)
    x, src, dst, edge_attr_32 = _rec_inputs()

    def _L0_gnn_setup():
        import jax, jax.numpy as jnp
        import numpy as np
        N, E = (50000, 25000)
        DIN = DOUT = 96
        DE = 32

        def _egnn_conv(x, src, dst, edge_attr, W_msg, W_edge, W_root, b):
            msg = x[src] @ W_msg + edge_attr @ W_edge
            agg = jax.ops.segment_max(msg, dst, num_segments=x.shape[0])
            agg = jnp.where(jnp.isneginf(agg), 0.0, agg)
            return agg + x @ W_root + b
        key = jax.random.key(seed)
        ks = jax.random.split(key, 10)
        rn = lambda k, sh, sc: jax.random.normal(k, sh, jnp.float32) * sc
        return {'X': rn(ks[0], (N, DIN), 1.0), 'edge_index': jax.random.randint(ks[1], (2, E), 0, N, jnp.int32), 'edge_attr': rn(ks[2], (E, DE), 1.0), 'W1_msg': rn(ks[3], (DIN, DOUT), DIN ** (-0.5)), 'W1_edge': rn(ks[4], (DE, DOUT), DE ** (-0.5)), 'W1_root': rn(ks[5], (DIN, DOUT), DIN ** (-0.5)), 'b1': jnp.zeros((DOUT,), jnp.float32), 'W2_msg': rn(ks[6], (DOUT, DOUT), DOUT ** (-0.5)), 'W2_edge': rn(ks[7], (DE, DOUT), DE ** (-0.5)), 'W2_root': rn(ks[8], (DOUT, DOUT), DOUT ** (-0.5)), 'b2': jnp.zeros((DOUT,), jnp.float32)}
    _L0_gnn_all = _L0_gnn_setup()
    _L0_gnn_in = {k: v for k, v in _L0_gnn_all.items() if k in ('W1_msg', 'W1_edge', 'W1_root', 'b1', 'W2_msg', 'W2_edge', 'W2_root', 'b2')}
    del _L0_gnn_all
    return {'x': x, 'src': src, 'dst': dst, 'edge_attr_32': edge_attr_32, 'L0_gnn_W1_msg': _L0_gnn_in['W1_msg'], 'L0_gnn_W1_edge': _L0_gnn_in['W1_edge'], 'L0_gnn_W1_root': _L0_gnn_in['W1_root'], 'L0_gnn_b1': _L0_gnn_in['b1'], 'L0_gnn_W2_msg': _L0_gnn_in['W2_msg'], 'L0_gnn_W2_edge': _L0_gnn_in['W2_edge'], 'L0_gnn_W2_root': _L0_gnn_in['W2_root'], 'L0_gnn_b2': _L0_gnn_in['b2']}

def reference(x, src, dst, edge_attr_32, L0_gnn_W1_msg, L0_gnn_W1_edge, L0_gnn_W1_root, L0_gnn_b1, L0_gnn_W2_msg, L0_gnn_W2_edge, L0_gnn_W2_root, L0_gnn_b2):
    import jax
    import jax.numpy as jnp

    def _L0_gnn_ref(X, edge_index, edge_attr, W1_msg, W1_edge, W1_root, b1, W2_msg, W2_edge, W2_root, b2):
        import jax, jax.numpy as jnp
        import numpy as np
        N, E = (50000, 25000)
        DIN = DOUT = 96
        DE = 32

        def _egnn_conv(x, src, dst, edge_attr, W_msg, W_edge, W_root, b):
            msg = x[src] @ W_msg + edge_attr @ W_edge
            agg = jax.ops.segment_max(msg, dst, num_segments=x.shape[0])
            agg = jnp.where(jnp.isneginf(agg), 0.0, agg)
            return agg + x @ W_root + b
        src, dst = (edge_index[0], edge_index[1])
        c1 = jax.nn.leaky_relu(_egnn_conv(X, src, dst, edge_attr, W1_msg, W1_edge, W1_root, b1))
        c2 = jax.nn.leaky_relu(_egnn_conv(c1, src, dst, edge_attr, W2_msg, W2_edge, W2_root, b2))
        return c2
    edge_index = jnp.stack([src, dst])
    x = _layernorm(x + _L0_gnn_ref(x, edge_index, edge_attr_32, L0_gnn_W1_msg, L0_gnn_W1_edge, L0_gnn_W1_root, L0_gnn_b1, L0_gnn_W2_msg, L0_gnn_W2_edge, L0_gnn_W2_root, L0_gnn_b2), axis=-1)
    return x

_drawn_inputs = setup_inputs


def setup_inputs(seed=0):
    import zlib

    import numpy as np

    out = dict(_drawn_inputs(seed))
    spreads = {'L0_gnn_b1': (0.0, 0.1), 'L0_gnn_b2': (0.0, 0.1)}
    factors = {}
    for name, (base, spread) in spreads.items():
        noise = np.random.default_rng([zlib.crc32(name.encode()), seed]).standard_normal(out[name].shape)
        drawn = base * np.exp(spread * noise) if base else spread * noise
        out[name] = jnp.asarray(drawn.astype(out[name].dtype))
    for name, factor in factors.items():
        out[name] = (out[name] * factor).astype(out[name].dtype)
    return out
```

```python
from contextlib import ExitStack

import concourse.bass as bass
from concourse import mybir

NODES = 50000
EDGES = 50000
D = 96
DE = 32
P = 128
U = 4
GROUP = P * U
GROUPS = -(-NODES // GROUP)
LAST_PARTS = (NODES - (GROUPS - 1) * GROUP) // U
ROW = D + 1
SLOTS = 4
LOOPS = GROUPS // SLOTS
COLS = GROUPS * U
HP = 125
HT = EDGES // HP
SLOPE = 0.01
EPS = 1e-5
BARRED = -3.3895e38

assert EDGES == NODES and HP * HT == EDGES and LAST_PARTS * U + (GROUPS - 1) * GROUP == NODES


class Group:

    def __init__(self, i, j):
        self.i, self.j = i, j
        self.index = i * SLOTS + j if not isinstance(i, int) else i * SLOTS + j
        self.static = isinstance(i, int)
        self.slot = j % SLOTS
        self.pair = j % 2
        self.parts = LAST_PARTS if self.static and self.index == GROUPS - 1 else P
        self.width = self.parts * U
        self.start = self.index * GROUP
        self.round = i + j // SLOTS
        self.pair_round = i * 2 + j // 2

    def back(self, n):
        if self.static and self.index < n:
            return None
        return Group(self.i, self.j - n)


def each_group(eng, body):
    for j in range(SLOTS):
        body(Group(0, j))
    with eng.Fori(1, LOOPS) as i:
        for j in range(SLOTS):
            body(Group(i, j))
    for j in range(LOOPS * SLOTS, GROUPS):
        body(Group(0, j))


def build_gnn(nc, x, src, dst, attr, w1_msg, w1_edge, w1_root, b1, w2_msg, w2_edge, w2_root, b2, out):
    f32, bf16 = mybir.dt.float32, mybir.dt.bfloat16
    i32, i16 = mybir.dt.int32, mybir.dt.int16
    ALU, ACT, AX = mybir.AluOpType, mybir.ActivationFunctionType, mybir.AxisListType

    node_table = nc.dram_tensor("node_table", (NODES, ROW), f32, kind="Internal").ap()
    barred = nc.dram_tensor("barred", (EDGES,), bf16, kind="Internal").ap()
    maxima = nc.dram_tensor("maxima", (EDGES + P, 2 * D), f32, kind="Internal").ap()
    src_side = nc.dram_tensor("src_side", (GROUPS, P, GROUP), f32, kind="Internal").ap()
    maxima_halves = maxima.rearrange("e (h d) -> (e h) d", h=2)

    def group_rows(array, g):
        return array[bass.ds(g.start, g.width), :].rearrange("(p u) d -> p u d", u=U)

    with ExitStack() as ctx:
        def make(stack):
            def sb(name, shape, dt=f32):
                return stack.enter_context(nc.sbuf_tensor(name, shape, dt))

            def ps(name, shape, dt=f32):
                return stack.enter_context(nc.psum_tensor(name, shape, dt))

            def sem(name):
                return stack.enter_context(nc.semaphore(name))
            return sb, ps, sem

        sb, ps, sem = make(ctx)
        ident = sb("ident", [P, P])
        w1 = sb("w1", [P, D])
        w2 = sb("w2", [P, D])
        root1 = sb("root1", [D, D])
        root2 = sb("root2", [D + 1, D])
        bias1 = sb("bias1", [D, 1])
        node_last = sb("node_last", [P, COLS], i32)
        src_last = sb("src_last", [P, COLS], i32)
        ident_ready = sem("ident_ready")
        weights_loaded = sem("weights_loaded")

        with ExitStack() as phase:
            sb, ps, sem = make(phase)
            XB = 8
            table = sb("table", [P, GROUPS, U, ROW])
            dst_i = sb("dst_i", [HP, HT], i32)
            dst_prev = sb("dst_prev", [HP, HT], i32)
            bar = sb("bar", [HP, HT], bf16)
            code_a = sb("code_a", [HP, HT], i32)
            code_b = sb("code_b", [HP, HT], i32)
            code_c = sb("code_c", [HP, HT], i32)
            row_code = sb("row_code", [HP, HT])
            col_code = sb("col_code", [HP, HT])
            iota = sb("iota", [P, COLS], i16)
            rows_hot = [sb(f"rows_hot{n}", [HP, P], bf16) for n in range(4)]
            cols_hot = [sb(f"cols_hot{n}", [HP, COLS], bf16) for n in range(4)]
            before = sb("before", [P, P])
            ones = sb("ones", [P, P])
            zero = sb("zero", [P, 2 * D])
            none_i = sb("none_i", [P, 1], i32)
            none = sb("none", [P, 1])
            none1 = sb("none1", [P, 1])
            counts = sb("counts", [P, GROUPS, U])
            row_sum = sb("row_sum", [P, GROUPS])
            total = sb("total", [P, GROUPS])
            zeros = sb("zeros", [P, GROUPS])
            running = sb("running", [P, GROUPS])
            base = sb("base", [P, GROUPS])
            cum = sb("cum", [P, GROUPS, U])
            filled = sb("filled", [P, GROUPS, U])
            hist = ps("hist", [P, COLS])
            sums = ps("sums", [P, 2, GROUPS])

            x_loaded, dst_loaded = sem("x_loaded"), sem("dst_loaded")
            bar_ready, bar_stored = sem("bar_ready"), sem("bar_stored")
            made, step = sem("made"), sem("step")
            hot_ready, hot_used = sem("hot_ready"), sem("hot_used")
            counted, sums_ready, row_sums = sem("counted"), sem("sums_ready"), sem("row_sums")
            table_ready, table_stored = sem("table_ready"), sem("table_stored")
            filled_in = sem("filled_in")
            block = phase.enter_context(nc.Block())

            whole = GROUPS - 1
            batches = [(g, min(XB, whole - g), P) for g in range(0, whole, XB)] + [(whole, 1, LAST_PARTS)]

            @block.sync
            def _(sp):
                sp.dma_start(dst_i[:, :], dst.rearrange("(p t) -> p t", t=HT)).then_inc(dst_loaded, 16)
                sp.dma_start(dst_prev[1:HP, :], dst[HT - 1:EDGES - 1].rearrange("(p t) -> p t", t=HT))\
                    .then_inc(dst_loaded, 16)
                sp.dma_start(dst_prev[0:1, 1:HT], dst[0:HT - 1].rearrange("(p t) -> p t", p=1))\
                    .then_inc(dst_loaded, 16)
                with sp.Fori(0, whole) as g:
                    sp.dma_start(table[:, bass.ds(g, 1), :, 1:ROW].rearrange("p g u d -> p (g u) d"),
                                 x[bass.ds(g * GROUP, GROUP), :].rearrange("(p u) d -> p u d", u=U))\
                        .then_inc(x_loaded, 16)
                sp.dma_start(table[0:LAST_PARTS, whole, :, 1:ROW],
                             x[whole * GROUP:NODES, :].rearrange("(p u) d -> p u d", u=U)).then_inc(x_loaded, 16)
                sp.wait_ge(bar_ready, 1)
                sp.dma_start(barred.rearrange("(p t) -> p t", t=HT), bar[:, :]).then_inc(bar_stored, 16)
                sp.wait_ge(made, 1)
                sp.dma_start(maxima[EDGES:EDGES + P, :], zero[:, :]).then_inc(table_stored, 16)
                sp.wait_ge(table_ready, 1)
                for g, n, parts in batches:
                    rows = node_table[g * GROUP:g * GROUP + n * parts * U, :]
                    sp.dma_start(rows.rearrange("(g p u) d -> p g (u d)", g=n, u=U),
                                 table[0:parts, g:g + n, :, :].rearrange("p g u d -> p g (u d)"))\
                        .then_inc(table_stored, 16)
                sp.wait_ge(bar_stored, 16)
                sp.wait_ge(table_stored, 16 * (1 + len(batches)))

            @block.scalar
            def _(act):
                for to, what in ((w1[0:D, :], w1_msg), (w1[D:P, :], w1_edge), (w2[0:D, :], w2_msg),
                                 (w2[D:P, :], w2_edge), (root1[:, :], w1_root), (root2[0:D, :], w2_root)):
                    act.dma_start(to, what[:, :]).then_inc(weights_loaded, 16)
                act.dma_start(bias1[:, :], b1.rearrange("(d o) -> d o", o=1)).then_inc(weights_loaded, 16)
                act.dma_start(root2[D:D + 1, :], b2.rearrange("(o d) -> o d", o=1)).then_inc(weights_loaded, 16)
                act.wait_ge(weights_loaded, 16 * 8)

            @block.gpsimd
            def _(pool):
                nc.gpsimd.memset(zero[:, :], 0.0).then_inc(made, 1)
                nc.gpsimd.iota(iota[:, :], pattern=[[1, COLS]], base=0, channel_multiplier=0,
                               allow_small_or_imprecise_dtypes=True).then_inc(filled_in, 1)
                nc.gpsimd.iota(none_i[:, :], pattern=[[0, 1]], base=EDGES, channel_multiplier=1)\
                    .then_inc(filled_in, 1)
                nc.gpsimd.memset(src_last[:, :], 0).then_inc(filled_in, 1)
                nc.gpsimd.memset(ident[:, :], 0.0).then_inc(filled_in, 1)
                nc.gpsimd.memset(before[:, :], 1.0).then_inc(filled_in, 1)
                nc.gpsimd.memset(ones[:, :], 1.0).then_inc(filled_in, 1)
                pool.wait_ge(filled_in, 6)
                nc.gpsimd.affine_select(out=ident[:, :], in_=ident[:, :], compare_op=ALU.not_equal, fill=1.0,
                                        base=0, pattern=[[-1, P]], channel_multiplier=1).then_inc(ident_ready, 1)
                nc.gpsimd.affine_select(out=before[:, :], in_=before[:, :], compare_op=ALU.is_gt, fill=0.0,
                                        base=0, pattern=[[1, P]], channel_multiplier=-1).then_inc(ident_ready, 1)

            @block.vector
            def _(dve):
                done = [0]

                def chain(instruction):
                    done[0] += 1
                    instruction.then_inc(step, 1)
                    dve.wait_ge(step, done[0])

                v = nc.vector
                chain(v.memset(dst_prev[0:1, 0:1], -1))
                v.memset(zeros[:, :], 0.0)
                dve.wait_ge(dst_loaded, 48)
                v.tensor_scalar(code_a[:, :], dst_i[:, :], 2, P - 1, ALU.logical_shift_right, ALU.bitwise_and)
                v.tensor_scalar(code_b[:, :], dst_i[:, :], 9, 2, ALU.logical_shift_right, ALU.logical_shift_left)
                chain(v.tensor_scalar(code_c[:, :], dst_i[:, :], U - 1, None, ALU.bitwise_and))
                v.tensor_copy(row_code[:, :], code_a[:, :])
                chain(v.tensor_tensor(col_code[:, :], code_b[:, :], code_c[:, :], ALU.add))
                dve.wait_ge(filled_in, 5)

                def one_hots(t, slot, wait):
                    if wait is not None:
                        dve.wait_ge(hot_used, wait)
                    v.tensor_scalar(rows_hot[slot][:, :], iota[0:HP, 0:P], row_code[:, bass.ds(t, 1)], None,
                                    ALU.is_equal)
                    v.tensor_scalar(cols_hot[slot][:, :], iota[0:HP, :], col_code[:, bass.ds(t, 1)], None,
                                    ALU.is_equal).then_inc(hot_ready, 1)

                for t in range(4):
                    one_hots(t, t, None)
                with dve.Fori(1, HT // 4) as i:
                    for k in range(4):
                        one_hots(i * 4 + k, k, i * 4 + k - 3)

                chain(v.tensor_tensor(dst_prev[:, :], dst_i[:, :], dst_prev[:, :], ALU.not_equal))
                v.tensor_scalar(bar[:, :], dst_prev[:, :], BARRED, None, ALU.mult).then_inc(bar_ready, 1)
                v.tensor_copy(none[:, :], none_i[:, :])
                dve.wait_ge(counted, 1)
                chain(v.tensor_copy(counts[:, :, :], hist[:, :].rearrange("p (g u) -> p g u", u=U)))
                v.tensor_reduce(row_sum[:, :], counts[:, :, :], AX.X, ALU.add).then_inc(row_sums, 1)
                v.tensor_scalar(filled[:, :, :], counts[:, :, :], 0.0, None, ALU.is_gt)
                v.tensor_scalar(none1[:, :], none[:, :], 1.0, None, ALU.add)
                v.tensor_copy(cum[:, :, 0], counts[:, :, 0])
                dve.wait_ge(sums_ready, 1)
                chain(v.tensor_copy(total[:, :], sums[:, 1, :]))
                chain(v.tensor_tensor_scan(running[:, :], total[:, :], zeros[:, :], 0.0, ALU.add, ALU.add))
                chain(v.tensor_tensor(base[:, :], running[:, :], total[:, :], ALU.subtract))
                chain(v.tensor_tensor(base[:, :], base[:, :], sums[:, 0, :], ALU.add))
                chain(v.tensor_tensor(cum[:, :, 0], cum[:, :, 0], base[:, :], ALU.add))
                for u in range(1, U):
                    chain(v.tensor_tensor(cum[:, :, u], cum[:, :, u - 1], counts[:, :, u], ALU.add))
                chain(v.tensor_scalar(cum[:, :, :], cum[:, :, :], none1[:, 0:1], None, ALU.subtract))
                chain(v.tensor_tensor(cum[:, :, :], cum[:, :, :], filled[:, :, :], ALU.mult))
                chain(v.tensor_scalar(cum[:, :, :], cum[:, :, :], none[:, 0:1], None, ALU.add))
                v.tensor_copy(node_last[:, :].rearrange("p (g u) -> p g u", u=U), cum[:, :, :])
                dve.wait_ge(x_loaded, 16 * GROUPS)
                v.tensor_scalar(table[:, :, :, 0], cum[:, :, :], 2.0, None, ALU.mult).then_inc(table_ready, 1)

            @block.tensor
            def _(pe):
                def count(slot, ready, start, stop):
                    pe.wait_ge(hot_ready, ready)
                    return nc.tensor.matmul(hist[:, :], rows_hot[slot][:, :], cols_hot[slot][:, :],
                                            start=start, stop=stop)

                for t in range(4):
                    count(t, t + 1, t == 0, False).then_inc(hot_used, 1)
                with pe.Fori(1, HT // 4 - 1) as i:
                    for k in range(4):
                        count(k, i * 4 + k + 1, False, False).then_inc(hot_used, 1)
                for t in range(HT - 4, HT):
                    last = count(t % 4, t + 1, False, t == HT - 1).then_inc(hot_used, 1) if t < HT - 1 \
                        else count(t % 4, t + 1, False, True)
                last.then_inc(counted, 1)
                pe.wait_ge(ident_ready, 2)
                pe.wait_ge(row_sums, 1)
                nc.tensor.matmul(sums[:, 0, :], before[:, :], row_sum[:, :], start=True, stop=True)
                nc.tensor.matmul(sums[:, 1, :], ones[:, :], row_sum[:, :], start=True, stop=True)\
                    .then_inc(sums_ready, 1)

        with ExitStack() as edges:
            sb, ps, sem = make(edges)
            bars = sb("bars", [D, EDGES], bf16)
            bars_loaded = [sem("bars_head_loaded"), sem("bars_loaded")]
            HEAD = SLOTS * GROUP

            def running_maximum(v, dve, g, scan, messages):
                prev = g.back(1)
                first = 0.0 if prev is None else scan[prev.pair][:, GROUP - 1:GROUP]
                return v.tensor_tensor_scan(scan[g.pair][:, 0:g.width], bars[:, bass.ds(g.start, g.width)],
                                            messages[g.pair][:, 0:g.width], first, ALU.add, ALU.max)

            with ExitStack() as phase:
                sb, ps, sem = make(phase)
                WIDE = ROW + DE
                index = [sb(f"index{n}", [P, U], i32) for n in range(SLOTS)]
                item = [sb(f"item{n}", [P, U, WIDE]) for n in range(SLOTS)]
                feat = [sb(f"feat{n}", [P, GROUP]) for n in range(2)]
                scan = [sb(f"scan{n}", [D, GROUP]) for n in range(2)]
                side = [sb(f"side{n}", [D, GROUP]) for n in range(2)]
                rows = [sb(f"rows{n}", [P, U, 2 * D]) for n in range(2)]
                item_t = [ps(f"item_t{n}", [P, GROUP]) for n in range(2)]
                messages = [ps(f"messages{n}", [D, GROUP]) for n in range(2)]
                roots = [ps(f"roots{n}", [D, GROUP]) for n in range(2)]
                rows_t = [ps(f"rows_t{n}", [P, U, D]) for n in range(2)]
                index_loaded = [sem(f"index_loaded{n}") for n in range(SLOTS)]
                attr_loaded = [sem(f"attr_loaded{n}") for n in range(SLOTS)]
                gathered = [sem(f"gathered{n}") for n in range(SLOTS)]
                transposed, last_kept, feat_ready = sem("transposed"), sem("last_kept"), sem("feat_ready")
                messages_ready, roots_ready = sem("messages_ready"), sem("roots_ready")
                scanned, side_ready = sem("scanned"), sem("side_ready")
                rows_back, rows_ready = sem("rows_back"), sem("rows_ready")
                rows_stored = [sem(f"rows_stored{n}") for n in range(2)]
                side_stored = [sem(f"side_stored{n}") for n in range(2)]
                pool_step, halves_cleared = sem("pool_step"), sem("halves_cleared")
                block = phase.enter_context(nc.Block())

                @block.sync
                def _(sp):
                    def load(g):
                        if g.back(SLOTS):
                            sp.wait_ge(gathered[g.slot], g.round * 64)
                        sp.dma_start(index[g.slot][0:g.parts, :],
                                     src[bass.ds(g.start, g.width)].rearrange("(p u) -> p u", u=U))\
                            .then_inc(index_loaded[g.slot], 16)
                        if g.back(SLOTS):
                            sp.wait_ge(transposed, g.index - SLOTS + 1)
                        sp.dma_start(item[g.slot][0:g.parts, :, ROW:WIDE], group_rows(attr, g))\
                            .then_inc(attr_loaded[g.slot], 16)

                    def store(g):
                        if g.static and g.index == 0:
                            sp.wait_ge(halves_cleared, 2)
                        sp.wait_ge(side_ready, g.index + 1)
                        sp.dma_start(src_side[bass.ds(g.index, 1), 0:D, 0:g.width].rearrange("o p c -> (o p) c"),
                                     side[g.pair][:, 0:g.width]).then_inc(side_stored[g.pair], 16)
                        sp.dma_start(src_side[bass.ds(g.index, 1), D:P, 0:g.width].rearrange("o p c -> (o p) c"),
                                     feat[g.pair][D:P, 0:g.width]).then_inc(side_stored[g.pair], 16)
                        sp.wait_ge(rows_ready, g.index + 1)
                        sp.dma_start(group_rows(maxima, g), rows[g.pair][0:g.parts, :, :])\
                            .then_inc(rows_stored[g.pair], 16)

                    def body(g):
                        load(g)
                        if g.static and g.index == 0:
                            sp.dma_start(bars[:, 0:HEAD], barred[0:HEAD].partition_broadcast(D))\
                                .then_inc(bars_loaded[0], 16)
                            sp.dma_start(bars[:, HEAD:EDGES], barred[HEAD:EDGES].partition_broadcast(D))\
                                .then_inc(bars_loaded[1], 16)
                        if g.back(3):
                            store(g.back(3))

                    each_group(sp, body)
                    for j in range(GROUPS - 3, GROUPS):
                        store(Group(0, j))
                    for n in range(2):
                        sp.wait_ge(rows_stored[n], 16 * (GROUPS // 2))
                        sp.wait_ge(side_stored[n], 32 * (GROUPS // 2))

                @block.gpsimd
                def _(pool):
                    for n in range(2):
                        nc.gpsimd.memset(rows[n][:, :, D:2 * D], 0.0).then_inc(halves_cleared, 1)

                    def body(g):
                        pool.wait_ge(index_loaded[g.slot], (g.round + 1) * 16)
                        if g.back(SLOTS):
                            pool.wait_ge(transposed, g.index - SLOTS + 1)
                            pool.wait_ge(last_kept, g.index - SLOTS + 1)
                        pool.sem_inc(pool_step, 1)
                        for u in range(U):
                            nc.gpsimd.indirect_dma_start(
                                item[g.slot][0:g.parts, u, 0:ROW], None, node_table[:, :],
                                bass.IndirectOffsetOnAxis(ap=index[g.slot][0:g.parts, u:u + 1], axis=0),
                            ).then_inc(gathered[g.slot], 16)

                    each_group(pool, body)

                @block.tensor
                def _(pe):
                    def arrive(g):
                        pe.wait_ge(gathered[g.slot], (g.round + 1) * 64)
                        pe.wait_ge(attr_loaded[g.slot], (g.round + 1) * 16)
                        if g.back(2):
                            pe.wait_ge(feat_ready, g.index - 1)
                        for u in range(U):
                            last = nc.tensor.transpose(item_t[g.pair][:, u:g.width:U], item[g.slot][0:g.parts, u, 1:WIDE],
                                                       ident[0:g.parts, 0:g.parts])
                        last.then_inc(transposed, 1)

                    def products(g):
                        pe.wait_ge(feat_ready, g.index + 1)
                        if g.back(2):
                            pe.wait_ge(scanned, g.index - 1)
                        nc.tensor.matmul(messages[g.pair][:, 0:g.width], w1[:, :], feat[g.pair][:, 0:g.width],
                                         start=True, stop=True).then_inc(messages_ready, 1)
                        if g.back(2):
                            pe.wait_ge(side_ready, g.index - 1)
                        nc.tensor.matmul(roots[g.pair][:, 0:g.width], root1[:, :], feat[g.pair][0:D, 0:g.width],
                                         start=True, stop=True).then_inc(roots_ready, 1)

                    def go_back(g):
                        pe.wait_ge(scanned, g.index + 1)
                        if g.back(2):
                            pe.wait_ge(rows_ready, g.index - 1)
                        for u in range(U):
                            last = nc.tensor.transpose(rows_t[g.pair][0:g.parts, u, :], scan[g.pair][:, u:g.width:U],
                                                       ident[0:D, 0:D])
                        last.then_inc(rows_back, 1)

                    def body(g):
                        arrive(g)
                        if g.back(1):
                            go_back(g.back(1))
                        products(g)

                    each_group(pe, body)
                    go_back(Group(0, GROUPS - 1))

                @block.vector
                def _(dve):
                    v = nc.vector

                    def body(g):
                        dve.wait_ge(gathered[g.slot], (g.round + 1) * 64)
                        v.tensor_copy(src_last[0:g.parts, bass.ds(g.index * U, U)], item[g.slot][0:g.parts, :, 0])\
                            .then_inc(last_kept, 1)
                        dve.wait_ge(transposed, g.index + 1)
                        if g.back(2):
                            dve.wait_ge(roots_ready, g.index - 1)
                            dve.wait_ge(side_stored[g.pair], g.pair_round * 32)
                        v.tensor_copy(feat[g.pair][:, 0:g.width], item_t[g.pair][:, 0:g.width]).then_inc(feat_ready, 1)
                        if g.static and g.index in (0, SLOTS):
                            dve.wait_ge(bars_loaded[0], 16)
                        dve.wait_ge(messages_ready, g.index + 1)
                        if g.back(1):
                            dve.wait_ge(scanned, g.index)
                        if g.back(2):
                            dve.wait_ge(rows_back, g.index - 1)
                        running_maximum(v, dve, g, scan, messages).then_inc(scanned, 1)
                        if g.static and g.index == SLOTS - 1:
                            dve.wait_ge(bars_loaded[1], 16)

                    each_group(dve, body)

                @block.scalar
                def _(act):
                    s = nc.scalar

                    def sides(g):
                        act.wait_ge(roots_ready, g.index + 1)
                        if g.back(2):
                            act.wait_ge(side_stored[g.pair], g.pair_round * 32)
                        s.activation(side[g.pair][:, 0:g.width], roots[g.pair][:, 0:g.width], ACT.Identity,
                                     bias=bias1[:, :]).then_inc(side_ready, 1)

                    def row_copy(g):
                        act.wait_ge(rows_back, g.index + 1)
                        if g.back(2):
                            act.wait_ge(rows_stored[g.pair], g.pair_round * 16)
                        s.activation(rows[g.pair][0:g.parts, :, 0:D], rows_t[g.pair][0:g.parts, :, :], ACT.Copy)\
                            .then_inc(rows_ready, 1)

                    def body(g):
                        if g.back(1):
                            row_copy(g.back(1))
                        sides(g)

                    each_group(act, body)
                    row_copy(Group(0, GROUPS - 1))

            with ExitStack() as phase:
                sb, ps, sem = make(phase)
                index = [sb(f"index_b{n}", [P, U], i32) for n in range(SLOTS)]
                item = [sb(f"item_b{n}", [P, U, D]) for n in range(SLOTS)]
                feat = [sb(f"feat_b{n}", [P, GROUP]) for n in range(SLOTS)]
                scan = [sb(f"scan_b{n}", [D, GROUP]) for n in range(2)]
                rows = [sb(f"rows_b{n}", [P, U, D]) for n in range(2)]
                item_t = [ps(f"item_tb{n}", [D, GROUP]) for n in range(2)]
                messages = [ps(f"messages_b{n}", [D, GROUP]) for n in range(2)]
                rows_t = [ps(f"rows_tb{n}", [P, U, D]) for n in range(2)]
                index_ready = sem("index_ready")
                side_loaded = [sem(f"side_loaded{n}") for n in range(SLOTS)]
                gathered = [sem(f"gathered_b{n}") for n in range(SLOTS)]
                transposed, summed, feat_ready = sem("transposed_b"), sem("summed"), sem("feat_ready_b")
                messages_ready, scanned = sem("messages_ready_b"), sem("scanned_b")
                rows_back, rows_ready = sem("rows_back_b"), sem("rows_ready_b")
                rows_stored = [sem(f"rows_stored_b{n}") for n in range(2)]
                pool_step = sem("pool_step_b")
                block = phase.enter_context(nc.Block())

                @block.sync
                def _(sp):
                    def load(g):
                        if g.back(SLOTS):
                            sp.wait_ge(messages_ready, g.index - SLOTS + 1)
                        sp.dma_start(feat[g.slot][:, 0:g.width],
                                     src_side[bass.ds(g.index, 1), :, 0:g.width].rearrange("o p c -> (o p) c"))\
                            .then_inc(side_loaded[g.slot], 16)

                    def store(g):
                        sp.wait_ge(rows_ready, g.index + 1)
                        sp.dma_start(group_rows(maxima[:, D:2 * D], g), rows[g.pair][0:g.parts, :, :])\
                            .then_inc(rows_stored[g.pair], 16)

                    def body(g):
                        load(g)
                        if g.back(3):
                            store(g.back(3))

                    each_group(sp, body)
                    for j in range(GROUPS - 3, GROUPS):
                        store(Group(0, j))
                    for n in range(2):
                        sp.wait_ge(rows_stored[n], 16 * (GROUPS // 2))

                @block.gpsimd
                def _(pool):
                    def body(g):
                        pool.wait_ge(index_ready, g.index + 1)
                        if g.back(SLOTS):
                            pool.wait_ge(transposed, g.index - SLOTS + 1)
                        pool.sem_inc(pool_step, 1)
                        for u in range(U):
                            nc.gpsimd.indirect_dma_start(
                                item[g.slot][0:g.parts, u, :], None, maxima_halves[:, :],
                                bass.IndirectOffsetOnAxis(ap=index[g.slot][0:g.parts, u:u + 1], axis=0),
                            ).then_inc(gathered[g.slot], 16)

                    each_group(pool, body)

                @block.tensor
                def _(pe):
                    def arrive(g):
                        pe.wait_ge(gathered[g.slot], (g.round + 1) * 64)
                        if g.back(2):
                            pe.wait_ge(summed, g.index - 1)
                        for u in range(U):
                            last = nc.tensor.transpose(item_t[g.pair][:, u:g.width:U], item[g.slot][0:g.parts, u, :],
                                                       ident[0:g.parts, 0:g.parts])
                        last.then_inc(transposed, 1)

                    def products(g):
                        pe.wait_ge(feat_ready, g.index + 1)
                        if g.back(2):
                            pe.wait_ge(scanned, g.index - 1)
                        nc.tensor.matmul(messages[g.pair][:, 0:g.width], w2[:, :], feat[g.slot][:, 0:g.width],
                                         start=True, stop=True).then_inc(messages_ready, 1)

                    def go_back(g):
                        pe.wait_ge(scanned, g.index + 1)
                        if g.back(2):
                            pe.wait_ge(rows_ready, g.index - 1)
                        for u in range(U):
                            last = nc.tensor.transpose(rows_t[g.pair][0:g.parts, u, :], scan[g.pair][:, u:g.width:U],
                                                       ident[0:D, 0:D])
                        last.then_inc(rows_back, 1)

                    def body(g):
                        arrive(g)
                        if g.back(1):
                            go_back(g.back(1))
                        products(g)

                    each_group(pe, body)
                    go_back(Group(0, GROUPS - 1))

                @block.vector
                def _(dve):
                    v = nc.vector

                    def take_index(g):
                        if g.back(SLOTS):
                            dve.wait_ge(gathered[g.slot], g.round * 64)
                        v.tensor_scalar(index[g.slot][0:g.parts, :], src_last[0:g.parts, bass.ds(g.index * U, U)],
                                        0, None, ALU.add).then_inc(index_ready, 1)

                    def body(g, ahead=True):
                        if g.static and g.index == 0:
                            for j in range(2):
                                take_index(Group(0, j))
                        if not (g.static and g.index + 2 >= GROUPS):
                            take_index(g.back(-2))
                        dve.wait_ge(transposed, g.index + 1)
                        dve.wait_ge(side_loaded[g.slot], (g.round + 1) * 16)
                        v.tensor_tensor(feat[g.slot][0:D, 0:g.width], item_t[g.pair][:, 0:g.width],
                                        feat[g.slot][0:D, 0:g.width], ALU.add).then_inc(summed, 1)
                        dve.wait_ge(summed, g.index + 1)
                        v.scalar_tensor_tensor(out=feat[g.slot][0:D, 0:g.width], in0=feat[g.slot][0:D, 0:g.width],
                                               scalar=SLOPE, in1=feat[g.slot][0:D, 0:g.width],
                                               op0=ALU.mult, op1=ALU.max).then_inc(feat_ready, 1)
                        dve.wait_ge(messages_ready, g.index + 1)
                        if g.back(1):
                            dve.wait_ge(scanned, g.index)
                        if g.back(2):
                            dve.wait_ge(rows_back, g.index - 1)
                        running_maximum(v, dve, g, scan, messages).then_inc(scanned, 1)

                    each_group(dve, body)

                @block.scalar
                def _(act):
                    s = nc.scalar

                    def row_copy(g):
                        act.wait_ge(rows_back, g.index + 1)
                        if g.back(2):
                            act.wait_ge(rows_stored[g.pair], g.pair_round * 16)
                        s.activation(rows[g.pair][0:g.parts, :, :], rows_t[g.pair][0:g.parts, :, :], ACT.Copy)\
                            .then_inc(rows_ready, 1)

                    each_group(act, row_copy)

        with ExitStack() as phase:
            sb, ps, sem = make(phase)
            index = [sb(f"index_n{n}", [P, U], i32) for n in range(SLOTS)]
            item = [sb(f"item_n{n}", [P, U, 2 * D]) for n in range(SLOTS)]
            xs = [sb(f"xs{n}", [P, U, D]) for n in range(SLOTS)]
            x_cols = [sb(f"x_cols{n}", [D, GROUP]) for n in range(2)]
            c1 = [sb(f"c1_{n}", [D + 1, GROUP]) for n in range(2)]
            biased = [sb(f"biased{n}", [D, GROUP]) for n in range(2)]
            c2 = [sb(f"c2_{n}", [P, U, D]) for n in range(2)]
            y = [sb(f"y{n}", [P, U, D]) for n in range(2)]
            result = [sb(f"result{n}", [P, U, D]) for n in range(2)]
            stats = [sb(f"stats{n}", [P, U, 6]) for n in range(2)]
            mean_var = [sb(f"mean_var{n}", [P, U, 2]) for n in range(2)]
            std = [sb(f"std{n}", [P, U]) for n in range(2)]
            rstd = [sb(f"rstd{n}", [P, U]) for n in range(2)]
            eps = sb("eps", [P, 1])
            x_t = [ps(f"x_t{n}", [D, GROUP]) for n in range(2)]
            pre1 = [ps(f"pre1_{n}", [D, GROUP]) for n in range(2)]
            pre2 = [ps(f"pre2_{n}", [P, U, D]) for n in range(2)]
            index_ready = sem("index_ready_n")
            x_loaded = [sem(f"x_loaded_n{n}") for n in range(SLOTS)]
            gathered = [sem(f"gathered_n{n}") for n in range(SLOTS)]
            const_ready, x_transposed, x_ready = sem("const_ready"), sem("x_transposed"), sem("x_ready")
            pre1_ready, c1_ready = sem("pre1_ready"), sem("c1_ready")
            biased_ready, scaled_ready = sem("biased_ready"), sem("scaled_ready")
            pre2_ready, c2_ready = sem("pre2_ready"), sem("c2_ready")
            y_ready, stats_ready, var_ready = sem("y_ready"), sem("stats_ready"), sem("var_ready")
            std_ready, rstd_ready, result_ready = sem("std_ready"), sem("rstd_ready"), sem("result_ready")
            result_stored = [sem(f"result_stored{n}") for n in range(2)]
            pool_step, dve_step = sem("pool_step_n"), sem("dve_step")
            block = phase.enter_context(nc.Block())

            @block.sync
            def _(sp):
                def load(g):
                    if g.back(SLOTS):
                        sp.wait_ge(y_ready, g.index - SLOTS + 1)
                    sp.dma_start(xs[g.slot][0:g.parts, :, :], group_rows(x, g)).then_inc(x_loaded[g.slot], 16)

                def store(g):
                    sp.wait_ge(result_ready, g.index + 1)
                    sp.dma_start(group_rows(out, g), result[g.pair][0:g.parts, :, :])\
                        .then_inc(result_stored[g.pair], 16)

                def body(g):
                    load(g)
                    if g.back(3):
                        store(g.back(3))

                each_group(sp, body)
                for j in range(GROUPS - 3, GROUPS):
                    store(Group(0, j))
                for n in range(2):
                    sp.wait_ge(result_stored[n], 16 * (GROUPS // 2))

            @block.gpsimd
            def _(pool):
                def body(g):
                    pool.wait_ge(index_ready, g.index + 1)
                    if g.back(SLOTS):
                        pool.wait_ge(pre2_ready, g.index - SLOTS + 1)
                    pool.sem_inc(pool_step, 1)
                    for u in range(U):
                        nc.gpsimd.indirect_dma_start(
                            item[g.slot][0:g.parts, u, :], None, maxima[:, :],
                            bass.IndirectOffsetOnAxis(ap=index[g.slot][0:g.parts, u:u + 1], axis=0),
                        ).then_inc(gathered[g.slot], 16)

                each_group(pool, body)

            @block.tensor
            def _(pe):
                def x_columns(g):
                    pe.wait_ge(x_loaded[g.slot], (g.round + 1) * 16)
                    if g.back(2):
                        pe.wait_ge(x_ready, g.index - 1)
                    for u in range(U):
                        last = nc.tensor.transpose(x_t[g.pair][:, u:g.width:U], xs[g.slot][0:g.parts, u, :],
                                                   ident[0:g.parts, 0:g.parts])
                    last.then_inc(x_transposed, 1)

                def layer1(g):
                    pe.wait_ge(x_ready, g.index + 1)
                    if g.back(2):
                        pe.wait_ge(biased_ready, g.index - 1)
                    nc.tensor.matmul(pre1[g.pair][:, 0:g.width], root1[:, :], x_cols[g.pair][:, 0:g.width],
                                     start=True, stop=False)
                    pe.wait_ge(gathered[g.slot], (g.round + 1) * 64)
                    for u in range(U):
                        last = nc.tensor.matmul(pre1[g.pair][:, u:g.width:U], item[g.slot][0:g.parts, u, 0:D],
                                                ident[0:g.parts, 0:g.parts], start=False, stop=(u == U - 1))
                    last.then_inc(pre1_ready, 1)

                def layer2(g):
                    pe.wait_ge(c1_ready, g.index + 1)
                    if g.back(2):
                        pe.wait_ge(c2_ready, g.index - 1)
                    nc.tensor.matmul(pre2[g.pair][0:g.parts, :, :], ident[0:g.parts, 0:g.parts],
                                     item[g.slot][0:g.parts, :, D:2 * D], start=True, stop=False)
                    for u in range(U):
                        last = nc.tensor.matmul(pre2[g.pair][0:g.parts, u, :], c1[g.pair][:, u:g.width:U],
                                                root2[:, :], start=False, stop=(u == U - 1))
                    last.then_inc(pre2_ready, 1)

                def body(g):
                    x_columns(g)
                    if g.back(1):
                        layer2(g.back(1))
                    layer1(g)

                each_group(pe, body)
                layer2(Group(0, GROUPS - 1))

            @block.vector
            def _(dve):
                v = nc.vector

                def take_index(g):
                    if g.back(SLOTS):
                        dve.wait_ge(gathered[g.slot], g.round * 64)
                    v.tensor_scalar(index[g.slot][0:g.parts, :], node_last[0:g.parts, bass.ds(g.index * U, U)],
                                    0, None, ALU.add).then_inc(index_ready, 1)

                def leak1(g):
                    dve.wait_ge(biased_ready, g.index + 1)
                    if g.back(2):
                        dve.wait_ge(pre2_ready, g.index - 1)
                    v.scalar_tensor_tensor(out=c1[g.pair][0:D, 0:g.width], in0=biased[g.pair][:, 0:g.width],
                                           scalar=SLOPE, in1=biased[g.pair][:, 0:g.width],
                                           op0=ALU.mult, op1=ALU.max).then_inc(c1_ready, 1)

                def moments(g):
                    dve.wait_ge(scaled_ready, g.index + 1)
                    v.scalar_tensor_tensor(out=c2[g.pair][0:g.parts, :, :], in0=pre2[g.pair][0:g.parts, :, :],
                                           scalar=1.0, in1=c2[g.pair][0:g.parts, :, :],
                                           op0=ALU.mult, op1=ALU.max).then_inc(c2_ready, 1)
                    dve.wait_ge(c2_ready, g.index + 1)
                    if g.back(2):
                        dve.wait_ge(result_ready, g.index - 1)
                    v.tensor_tensor(y[g.pair][0:g.parts, :, :], c2[g.pair][0:g.parts, :, :],
                                    xs[g.slot][0:g.parts, :, :], ALU.add).then_inc(y_ready, 1)
                    dve.wait_ge(y_ready, g.index + 1)
                    for u in range(U):
                        last = v.bn_stats(stats[g.pair][0:g.parts, u, :], y[g.pair][0:g.parts, u, :])
                    last.then_inc(stats_ready, 1)
                    dve.wait_ge(stats_ready, g.index + 1)
                    dve.sem_inc(dve_step, 1)
                    for u in range(U):
                        last = v.bn_aggr(mean_var[g.pair][0:g.parts, u, :], stats[g.pair][0:g.parts, u, :])
                    last.then_inc(var_ready, 1)

                def normalize(g):
                    dve.wait_ge(std_ready, g.index + 1)
                    v.reciprocal(rstd[g.pair][0:g.parts, :], std[g.pair][0:g.parts, :]).then_inc(rstd_ready, 1)
                    dve.wait_ge(rstd_ready, g.index + 1)
                    if g.back(2):
                        dve.wait_ge(result_stored[g.pair], g.pair_round * 16)
                    for u in range(U):
                        last = v.tensor_scalar(result[g.pair][0:g.parts, u, :], y[g.pair][0:g.parts, u, :],
                                               mean_var[g.pair][0:g.parts, u, 0:1], rstd[g.pair][0:g.parts, u:u + 1],
                                               ALU.subtract, ALU.mult)
                    last.then_inc(result_ready, 1)

                def body(g):
                    if g.static and g.index == 0:
                        for j in range(2):
                            take_index(Group(0, j))
                    if not (g.static and g.index + 2 >= GROUPS):
                        take_index(g.back(-2))
                    leak1(g)
                    if g.back(2):
                        normalize(g.back(2))
                    if g.back(1):
                        moments(g.back(1))

                v.memset(eps[:, :], EPS).then_inc(const_ready, 1)
                for n in range(2):
                    v.memset(c1[n][D:D + 1, :], 1.0).then_inc(const_ready, 1)
                each_group(dve, body)
                normalize(Group(0, GROUPS - 2))
                moments(Group(0, GROUPS - 1))
                normalize(Group(0, GROUPS - 1))

            @block.scalar
            def _(act):
                s = nc.scalar

                def x_copy(g):
                    act.wait_ge(x_transposed, g.index + 1)
                    if g.back(2):
                        act.wait_ge(pre1_ready, g.index - 1)
                    s.activation(x_cols[g.pair][:, 0:g.width], x_t[g.pair][:, 0:g.width], ACT.Copy)\
                        .then_inc(x_ready, 1)

                def bias(g):
                    act.wait_ge(pre1_ready, g.index + 1)
                    if g.back(2):
                        act.wait_ge(c1_ready, g.index - 1)
                    s.activation(biased[g.pair][:, 0:g.width], pre1[g.pair][:, 0:g.width], ACT.Identity,
                                 bias=bias1[:, :]).then_inc(biased_ready, 1)

                def scale(g):
                    act.wait_ge(pre2_ready, g.index + 1)
                    if g.back(2):
                        act.wait_ge(y_ready, g.index - 1)
                    s.activation(c2[g.pair][0:g.parts, :, :], pre2[g.pair][0:g.parts, :, :], ACT.Copy,
                                 scale=SLOPE).then_inc(scaled_ready, 1)

                def root(g):
                    act.wait_ge(var_ready, g.index + 1)
                    if g.back(2):
                        act.wait_ge(rstd_ready, g.index - 1)
                    s.activation(std[g.pair][0:g.parts, :], mean_var[g.pair][0:g.parts, :, 1], ACT.Sqrt,
                                 bias=eps[0:g.parts, :]).then_inc(std_ready, 1)

                def body(g):
                    x_copy(g)
                    if g.back(2):
                        root(g.back(2))
                    if g.back(1):
                        scale(g.back(1))
                    bias(g)

                act.wait_ge(const_ready, 3)
                each_group(act, body)
                root(Group(0, GROUPS - 2))
                scale(Group(0, GROUPS - 1))
                root(Group(0, GROUPS - 1))


_INS = ["x", "src", "dst", "edge_attr_32", "L0_gnn_W1_msg", "L0_gnn_W1_edge", "L0_gnn_W1_root", "L0_gnn_b1",
        "L0_gnn_W2_msg", "L0_gnn_W2_edge", "L0_gnn_W2_root", "L0_gnn_b2"]


def kernel(**inputs):
    import numpy as _np
    import concourse.bacc as _bacc
    from concourse import mybir as _mybir
    from concourse.bass_utils import run_bass_kernel_spmd as _run

    nc = _bacc.Bacc("TRN2", target_bir_lowering=False, num_devices=1)
    arrays, args = {}, []
    for name in _INS:
        a = _np.ascontiguousarray(inputs[name])
        arrays[f"in_{name}"] = a
        args.append(nc.dram_tensor(f"in_{name}", a.shape, _mybir.dt.from_np(a.dtype), kind="ExternalInput").ap())
    args.append(nc.dram_tensor("out_0", (NODES, D), _mybir.dt.float32, kind="ExternalOutput").ap())
    build_gnn(nc, *args)
    return _run(nc, [arrays], core_ids=[0]).results[0]["out_0"]
```

```python
from contextlib import ExitStack

import concourse.bass as bass
from concourse import mybir

NODES = 50000
EDGES = 50000
D = 96
DE = 32
P = 128
U = 4
GROUP = P * U
GROUPS = -(-NODES // GROUP)
LAST_PARTS = (NODES - (GROUPS - 1) * GROUP) // U
SLOTS = 8
LOOPS = GROUPS // SLOTS
COLS = GROUPS * U
HP = 125
HT = EDGES // HP
HSTEPS = 8
HFIRST = 6
SPLIT = (HFIRST + HT // HSTEPS) // SLOTS
LOOKED1 = GROUPS - 1 - SPLIT * SLOTS + 1
ROWS2 = 2
COLS2 = COLS // ROWS2
SLOPE = 0.01
EPS = 1e-5
BARRED = -3.3895e38

assert EDGES == NODES and HP * HT == EDGES and LAST_PARTS * U + (GROUPS - 1) * GROUP == NODES
assert SPLIT * SLOTS == HFIRST + HT // HSTEPS and LOOKED1 + SPLIT * SLOTS == GROUPS


class Group:

    def __init__(self, i, j, late=False):
        self.i, self.j, self.late = i, j, late
        self.index = i * SLOTS + j
        self.static = isinstance(i, int)
        self.slot = j % SLOTS
        self.pair = j % 2
        self.quad = j % 4
        self.parts = LAST_PARTS if self.static and self.index == GROUPS - 1 else P
        self.width = self.parts * U
        self.start = self.index * GROUP
        self.round = i + j // SLOTS
        self.pair_round = i * (SLOTS // 2) + j // 2

    def back(self, n):
        if self.static and self.index < n:
            return None
        return Group(self.i, self.j - n, self.late)

    def on(self, n):
        if self.static and self.index + n >= GROUPS:
            return None
        return Group(self.i, self.j + n, self.late)


def each_group(eng, body, between=None):
    for j in range(SLOTS):
        body(Group(0, j))
    with eng.Fori(1, SPLIT) as i:
        for j in range(SLOTS):
            body(Group(i, j))
    if between:
        between()
    with eng.Fori(SPLIT, LOOPS) as i:
        for j in range(SLOTS):
            body(Group(i, j, True))
    for j in range(LOOPS * SLOTS, GROUPS):
        body(Group(0, j, True))


def build_gnn(nc, x, src, dst, attr, w1_msg, w1_edge, w1_root, b1, w2_msg, w2_edge, w2_root, b2, out):
    f32, bf16 = mybir.dt.float32, mybir.dt.bfloat16
    i32, i16 = mybir.dt.int32, mybir.dt.int16
    ALU, ACT, AX = mybir.AluOpType, mybir.ActivationFunctionType, mybir.AxisListType

    barred = nc.dram_tensor("barred", (EDGES,), bf16, kind="Internal").ap()
    src_rows = nc.dram_tensor("src_rows", (GROUPS * GROUP,), bf16, kind="Internal").ap()
    maxima = nc.dram_tensor("maxima", (EDGES + P, 2 * D), f32, kind="Internal").ap()
    src_side = nc.dram_tensor("src_side", (GROUPS, P, GROUP), f32, kind="Internal").ap()
    maxima_halves = maxima.rearrange("e (h d) -> (e h) d", h=2)

    def group_rows(array, g):
        return array[bass.ds(g.start, g.width), :].rearrange("(p u) d -> p u d", u=U)

    def side_of(g, first, last):
        return src_side[bass.ds(g.index, 1), first:last, 0:g.width].rearrange("o p c -> (o p) c")

    with ExitStack() as ctx:
        def make(stack):
            def sb(name, shape, dt=f32):
                return stack.enter_context(nc.sbuf_tensor(name, shape, dt))

            def ps(name, shape, dt=f32):
                return stack.enter_context(nc.psum_tensor(name, shape, dt))

            def sem(name):
                return stack.enter_context(nc.semaphore(name))
            return sb, ps, sem

        sb, ps, sem = make(ctx)
        ident = sb("ident", [P, P])
        w1 = sb("w1", [P, D])
        w2 = sb("w2", [P, D])
        root1 = sb("root1", [D, D])
        root2 = sb("root2", [D + 1, D])
        bias1 = sb("bias1", [D, 1])
        node_last = sb("node_last", [P, COLS], i32)
        node_index = [sb(f"node_index{n}", [P, U], i32) for n in range(SLOTS)]
        node_index_loaded = [sem(f"node_index_loaded{n}") for n in range(SLOTS)]

        def load_node_index(sp, g):
            sp.dma_start(node_index[g.slot][0:g.parts, :], node_last[0:g.parts, bass.ds(g.index * U, U)])\
                .then_inc(node_index_loaded[g.slot], 16)

        with ExitStack() as edges:
            sb, ps, sem = make(edges)
            bars = sb("bars", [D, EDGES], bf16)
            src_last = sb("src_last", [P, COLS + U])
            src_col = sb("src_col", [P, COLS])
            iota = sb("iota", [P, COLS], i16)
            row_of = sb("row_of", [P, ROWS2])
            high = sb("high", [P, GROUPS, U], bf16)
            low = sb("low", [P, GROUPS, U], bf16)
            src_row = [sb(f"src_row{n}", [P, GROUP], bf16) for n in range(SLOTS)]
            src_hot = sb("src_hot", [P, ROWS2, GROUP], bf16)
            unused = sb("unused", [P, U, COLS2])
            picked = ps("picked", [P, U, 256])
            src_row_loaded = [sem(f"src_row_loaded{n}") for n in range(SLOTS)]
            src_hot_ready, picked_ready, looked_up = sem("src_hot_ready"), sem("picked_ready"), sem("looked_up")

            def load_src_row(sp, m):
                sp.wait_ge(src_hot_ready, m.index + 1)
                sp.dma_start(src_row[m.slot][:, :], src_rows[bass.ds(m.start, GROUP)].partition_broadcast(P))\
                    .then_inc(src_row_loaded[m.slot], 16)

            def hot_rows(dve, m):
                dve.wait_ge(src_row_loaded[m.slot], (m.round + 1) * 16)
                if not m.static or m.index >= 1:
                    dve.wait_ge(picked_ready, m.index)
                for k in range(ROWS2):
                    last = nc.vector.tensor_scalar(src_hot[:, k, :], src_row[m.slot][:, :], row_of[:, k:k + 1],
                                                   None, ALU.is_equal)
                last.then_inc(src_hot_ready, 1)

            def pick_rows(pe, m):
                pe.wait_ge(src_hot_ready, SLOTS + m.index + 1)
                if not m.static or m.index >= 1:
                    pe.wait_ge(looked_up, m.index)
                for u in range(U):
                    for k in range(ROWS2):
                        for part in (high, low):
                            last = nc.tensor.matmul(picked[:, u, 0:COLS2], src_hot[:, k, u:GROUP:U],
                                                    part[:, k:GROUPS:ROWS2, :], start=(k == 0 and part is high),
                                                    stop=(k == ROWS2 - 1 and part is low))
                last.then_inc(picked_ready, 1)

            def pick_columns(dve, m):
                dve.wait_ge(picked_ready, m.index + 1)
                for u in range(U):
                    last = nc.vector.scalar_tensor_tensor(
                        out=unused[:, u, :], in0=iota[:, 0:COLS2], scalar=src_col[:, bass.ds(m.index * U + u, 1)],
                        in1=picked[:, u, 0:COLS2], op0=ALU.is_equal, op1=ALU.mult,
                        accum_out=src_last[:, bass.ds(m.index * U + u, 1)])
                last.then_inc(looked_up, 1)

            def running_maximum(g, scan, messages):
                prev = g.back(1)
                first = 0.0 if prev is None else scan[prev.pair][:, GROUP - 1:GROUP]
                return nc.vector.tensor_tensor_scan(scan[g.pair][:, 0:g.width], bars[:, bass.ds(g.start, g.width)],
                                                    messages[:, 0:g.width], first, ALU.add, ALU.max)

            with ExitStack() as phase:
                sb, ps, sem = make(phase)
                WIDE = D + DE
                index = [sb(f"index{n}", [P, U], i32) for n in range(SLOTS)]
                item = [sb(f"item{n}", [P, U, WIDE]) for n in range(SLOTS)]
                feat = [sb(f"feat{n}", [P, GROUP]) for n in range(2)]
                scan = [sb(f"scan{n}", [D, GROUP]) for n in range(2)]
                side = [sb(f"side{n}", [D, GROUP]) for n in range(2)]
                rows = [sb(f"rows{n}", [P, U, 2 * D]) for n in range(2)]
                item_t = [ps(f"item_t{n}", [P, GROUP]) for n in range(2)]
                messages = ps("messages", [D, GROUP])
                roots = ps("roots", [D, GROUP])
                rows_t = ps("rows_t", [P, U, D])
                index_loaded = [sem(f"index_loaded{n}") for n in range(SLOTS)]
                attr_loaded = [sem(f"attr_loaded{n}") for n in range(SLOTS)]
                bars_loaded = [sem(f"bars_loaded{n}") for n in range(SLOTS)]
                gathered = [sem(f"gathered{n}") for n in range(SLOTS)]
                transposed, feat_ready = sem("transposed"), sem("feat_ready")
                messages_ready, roots_ready = sem("messages_ready"), sem("roots_ready")
                scanned, side_ready = sem("scanned"), sem("side_ready")
                rows_back, rows_ready = sem("rows_back"), sem("rows_ready")
                rows_stored = [sem(f"rows_stored{n}") for n in range(2)]
                side_stored = [sem(f"side_stored{n}") for n in range(2)]
                pool_step, halves_cleared = sem("pool_step"), sem("halves_cleared")

                dst_i = sb("dst_i", [HP, HT], i32)
                dst_prev = sb("dst_prev", [HP, HT], i32)
                src_i = sb("src_i", [HP, HT], i32)
                src_all = sb("src_all", [P, COLS], i32)
                src_code = sb("src_code", [HP, HT], bf16)
                bar = sb("bar", [HP, HT], bf16)
                code_a = sb("code_a", [HP, HT], i32)
                code_b = sb("code_b", [HP, HT], i32)
                code_c = sb("code_c", [HP, HT], i32)
                part_a = sb("part_a", [P, COLS], i32)
                part_b = sb("part_b", [P, COLS], i32)
                row_code = sb("row_code", [HP, HT], bf16)
                col_code = sb("col_code", [HP, HT])
                iota_rows = sb("iota_rows", [HP, P, HSTEPS], bf16)
                rows_hot = [sb(f"rows_hot{n}", [HP, P, HSTEPS], bf16) for n in range(2)]
                cols_hot = [sb(f"cols_hot{n}", [HP, HSTEPS, COLS], bf16) for n in range(2)]
                before = sb("before", [P, P])
                ones = sb("ones", [P, P])
                zero = sb("zero", [P, 2 * D])
                none_i = sb("none_i", [P, 1], i32)
                none = sb("none", [P, 1])
                none1 = sb("none1", [P, 1])
                counts = sb("counts", [P, GROUPS, U])
                row_sum = sb("row_sum", [P, GROUPS])
                total = sb("total", [P, GROUPS])
                zeros = sb("zeros", [P, GROUPS])
                running = sb("running", [P, GROUPS])
                base = sb("base", [P, GROUPS])
                cum = sb("cum", [P, GROUPS, U])
                filled = sb("filled", [P, GROUPS, U])
                hist = ps("hist", [P, COLS])
                dst_loaded, src_loaded, src_all_loaded = sem("dst_loaded"), sem("src_loaded"), sem("src_all_loaded")
                weights_loaded = sem("weights_loaded")
                bar_ready, bar_stored = sem("bar_ready"), sem("bar_stored")
                code_ready, code_stored = sem("code_ready"), sem("code_stored")
                made, const_ready, ident_ready, step = sem("made"), sem("const_ready"), sem("ident_ready"), sem("step")
                hot_ready, hot_used = sem("hot_ready"), sem("hot_used")
                counted, sums_ready, row_sums = sem("counted"), sem("sums_ready"), sem("row_sums")
                sums_read, zero_stored = sem("sums_read"), sem("zero_stored")
                block = phase.enter_context(nc.Block())

                @block.sync
                def _(sp):
                    def load(g):
                        if g.back(SLOTS):
                            sp.wait_ge(gathered[g.slot], g.round * 64)
                        sp.dma_start(index[g.slot][0:g.parts, :],
                                     src[bass.ds(g.start, g.width)].rearrange("(p u) -> p u", u=U))\
                            .then_inc(index_loaded[g.slot], 16)
                        if g.static and g.index == 0:
                            sp.dma_start(dst_i[:, :], dst.rearrange("(p t) -> p t", t=HT)).then_inc(dst_loaded, 16)
                            sp.dma_start(dst_prev[1:HP, :], dst[HT - 1:EDGES - 1].rearrange("(p t) -> p t", t=HT))\
                                .then_inc(dst_loaded, 16)
                            sp.dma_start(dst_prev[0:1, 1:HT], dst[0:HT - 1].rearrange("(p t) -> p t", p=1))\
                                .then_inc(dst_loaded, 16)
                            sp.dma_start(src_i[:, :], src.rearrange("(p t) -> p t", t=HT)).then_inc(src_loaded, 16)
                        if g.back(SLOTS):
                            sp.wait_ge(transposed, g.index - SLOTS + 1)
                        sp.dma_start(item[g.slot][0:g.parts, :, D:WIDE], group_rows(attr, g))\
                            .then_inc(attr_loaded[g.slot], 16)

                    def load_bars(g):
                        if g.back(SLOTS):
                            sp.wait_ge(scanned, g.index - SLOTS + 1)
                        sp.dma_start(bars[:, bass.ds(g.start, g.width)],
                                     barred[bass.ds(g.start, g.width)].partition_broadcast(D))\
                            .then_inc(bars_loaded[g.slot], 16)

                    def body(g):
                        if not g.static or g.index >= SLOTS:
                            load(g)
                            load_bars(g)
                        elif g.index == 0:
                            for j in range(SLOTS):
                                load(Group(0, j))
                            sp.wait_ge(bar_stored, 16)
                            for j in range(SLOTS):
                                load_bars(Group(0, j))
                            whole = (GROUPS - 1) * GROUP
                            sp.dma_start(src_all[:, 0:COLS - U].rearrange("p (g u) -> p g u", u=U),
                                         src[0:whole].rearrange("(g p u) -> p g u", p=P, u=U))\
                                .then_inc(src_all_loaded, 16)
                            sp.wait_ge(const_ready, 6)
                            sp.dma_start(src_all[0:LAST_PARTS, COLS - U:COLS],
                                         src[whole:EDGES].rearrange("(p u) -> p u", u=U))\
                                .then_inc(src_all_loaded, 16)
                            sp.wait_ge(made, 1)
                            sp.dma_start(maxima[EDGES:EDGES + P, :], zero[:, :]).then_inc(zero_stored, 16)
                            sp.wait_ge(code_stored, 32)
                        if g.late and not (g.static and g.index == GROUPS - 1):
                            load_src_row(sp, Group(g.i, g.j - SPLIT * SLOTS + 1))

                    each_group(sp, body, between=lambda: load_src_row(sp, Group(0, 0)))
                    sp.wait_ge(zero_stored, 16)
                    for n in range(2):
                        sp.wait_ge(rows_stored[n], 16 * (GROUPS // 2))
                        sp.wait_ge(side_stored[n], 32 * (GROUPS // 2))

                @block.gpsimd
                def _(pool):
                    p = nc.gpsimd
                    p.memset(ident[:, :], 0.0).then_inc(const_ready, 1)
                    p.iota(iota[:, :], pattern=[[1, COLS]], base=0, channel_multiplier=0,
                           allow_small_or_imprecise_dtypes=True).then_inc(const_ready, 1)
                    p.iota(none_i[:, :], pattern=[[0, 1]], base=EDGES, channel_multiplier=1).then_inc(const_ready, 1)
                    p.memset(before[:, :], 1.0).then_inc(const_ready, 1)
                    p.memset(src_all[:, COLS - U:COLS], 0).then_inc(const_ready, 1)
                    p.memset(src_last[:, COLS:COLS + U], 0.0).then_inc(const_ready, 1)
                    pool.wait_ge(const_ready, 6)
                    p.affine_select(out=ident[:, :], in_=ident[:, :], compare_op=ALU.not_equal, fill=1.0,
                                    base=0, pattern=[[-1, P]], channel_multiplier=1).then_inc(ident_ready, 1)

                    def body(g):
                        pool.wait_ge(index_loaded[g.slot], (g.round + 1) * 16)
                        if g.back(SLOTS):
                            pool.wait_ge(transposed, g.index - SLOTS + 1)
                        pool.sem_inc(pool_step, 1)
                        for u in range(U):
                            p.indirect_dma_start(
                                item[g.slot][0:g.parts, u, 0:D], None, x[:, :],
                                bass.IndirectOffsetOnAxis(ap=index[g.slot][0:g.parts, u:u + 1], axis=0),
                            ).then_inc(gathered[g.slot], 16)
                        if g.static and g.index == 0:
                            p.affine_select(out=before[:, :], in_=before[:, :], compare_op=ALU.is_gt, fill=0.0,
                                            base=0, pattern=[[1, P]], channel_multiplier=-1).then_inc(ident_ready, 1)

                    each_group(pool, body)

                @block.tensor
                def _(pe):
                    def arrive(g):
                        pe.wait_ge(gathered[g.slot], (g.round + 1) * 64)
                        pe.wait_ge(attr_loaded[g.slot], (g.round + 1) * 16)
                        if g.back(2):
                            pe.wait_ge(feat_ready, g.index - 1)
                        for u in range(U):
                            last = nc.tensor.transpose(item_t[g.pair][:, u:g.width:U], item[g.slot][0:g.parts, u, :],
                                                       ident[0:g.parts, 0:g.parts])
                        last.then_inc(transposed, 1)

                    def products(g):
                        pe.wait_ge(feat_ready, g.index + 1)
                        if g.back(1):
                            pe.wait_ge(scanned, g.index)
                        nc.tensor.matmul(messages[:, 0:g.width], w1[:, :], feat[g.pair][:, 0:g.width],
                                         start=True, stop=True).then_inc(messages_ready, 1)
                        if g.back(1):
                            pe.wait_ge(side_ready, g.index)
                        nc.tensor.matmul(roots[:, 0:g.width], root1[:, :], feat[g.pair][0:D, 0:g.width],
                                         start=True, stop=True).then_inc(roots_ready, 1)

                    def go_back(g):
                        pe.wait_ge(scanned, g.index + 1)
                        if g.back(1):
                            pe.wait_ge(rows_ready, g.index)
                        for u in range(U):
                            last = nc.tensor.transpose(rows_t[0:g.parts, u, :], scan[g.pair][:, u:g.width:U],
                                                       ident[0:D, 0:D])
                        last.then_inc(rows_back, 1)

                    def count(b):
                        first = b.static and b.index == 0
                        for k in range(HSTEPS):
                            pe.wait_ge(hot_ready, b.index * HSTEPS + k + 1)
                            last = nc.tensor.matmul(hist[:, :], rows_hot[b.pair][:, :, k], cols_hot[b.pair][:, k, :],
                                                    start=(first and k == 0), stop=False, skip_group_check=True)
                        last.then_inc(hot_used, 1)

                    def body(g):
                        arrive(g)
                        if not g.late and g.back(HFIRST + 1):
                            count(g.back(HFIRST + 1))
                        if g.late and not (g.static and g.index == GROUPS - 1):
                            pick_rows(pe, Group(g.i, g.j - SPLIT * SLOTS))
                        if g.back(1):
                            go_back(g.back(1))
                        products(g)

                    def finish_counts():
                        count(Group(0, HT // HSTEPS - 1))
                        pe.wait_ge(ident_ready, 2)
                        pe.wait_ge(made, 2)
                        pe.wait_ge(row_sums, 1)
                        pe.wait_ge(rows_ready, SPLIT * SLOTS - 1)
                        two = rows_t[:, :, :].rearrange("p u d -> p (u d)")
                        nc.tensor.matmul(two[:, 0:GROUPS], before[:, :], row_sum[:, :], start=True, stop=True)
                        nc.tensor.matmul(two[:, GROUPS:2 * GROUPS], ones[:, :], row_sum[:, :], start=True, stop=True)\
                            .then_inc(sums_ready, 1)
                        pe.wait_ge(sums_read, 1)

                    pe.wait_ge(ident_ready, 1)
                    pe.wait_ge(weights_loaded, 16 * 8)
                    each_group(pe, body, between=finish_counts)
                    go_back(Group(0, GROUPS - 1))

                @block.vector
                def _(dve):
                    done = [0]

                    def chain(instruction):
                        done[0] += 1
                        instruction.then_inc(step, 1)
                        dve.wait_ge(step, done[0])

                    v = nc.vector
                    dve.sem_inc(src_hot_ready, SLOTS)
                    chain(v.memset(dst_prev[0:1, 0:1], -1))
                    v.memset(zeros[:, :], 0.0)
                    v.memset(zero[:, :], 0.0).then_inc(made, 1)
                    for n in range(2):
                        v.memset(rows[n][:, :, D:2 * D], 0.0).then_inc(halves_cleared, 1)
                    v.memset(ones[:, :], 1.0).then_inc(made, 1)
                    dve.wait_ge(dst_loaded, 48)
                    chain(v.tensor_tensor(dst_prev[:, :], dst_i[:, :], dst_prev[:, :], ALU.not_equal))
                    v.tensor_scalar(bar[:, :], dst_prev[:, :], BARRED, None, ALU.mult).then_inc(bar_ready, 1)
                    v.tensor_scalar(code_a[:, :], dst_i[:, :], 2, P - 1, ALU.logical_shift_right, ALU.bitwise_and)
                    v.tensor_scalar(code_b[:, :], dst_i[:, :], 9, 2, ALU.logical_shift_right, ALU.logical_shift_left)
                    chain(v.tensor_scalar(code_c[:, :], dst_i[:, :], U - 1, None, ALU.bitwise_and))
                    chain(v.tensor_copy(row_code[:, :], code_a[:, :]))
                    chain(v.tensor_tensor(col_code[:, :], code_b[:, :], code_c[:, :], ALU.add))
                    dve.wait_ge(src_loaded, 16)
                    chain(v.tensor_scalar(code_a[:, :], src_i[:, :], 2, ROWS2 * P - 1,
                                          ALU.logical_shift_right, ALU.bitwise_and))
                    v.tensor_copy(src_code[:, :], code_a[:, :]).then_inc(code_ready, 1)
                    dve.wait_ge(const_ready, 6)
                    chain(v.tensor_copy(none[:, :], none_i[:, :]))
                    v.tensor_scalar(none1[:, :], none[:, :], 1.0, None, ALU.add)
                    for k in range(HSTEPS):
                        v.tensor_copy(iota_rows[:, :, k], iota[0:HP, 0:P])
                    for k in range(ROWS2):
                        v.tensor_scalar(row_of[:, k:k + 1], none[:, :], float(k * P - EDGES), None, ALU.add)

                    def one_hots(b):
                        if b.back(2):
                            dve.wait_ge(hot_used, b.index - 1)
                        codes = row_code[:, bass.ds(b.index * HSTEPS, HSTEPS)]
                        v.tensor_tensor(rows_hot[b.pair][:, :, :], iota_rows[:, :, :],
                                        codes.unsqueeze(1).broadcast_to([HP, P, HSTEPS]), ALU.is_equal)
                        for k in range(HSTEPS):
                            v.tensor_scalar(cols_hot[b.pair][:, k, :], iota[0:HP, :],
                                            col_code[:, bass.ds(b.index * HSTEPS + k, 1)], None,
                                            ALU.is_equal).then_inc(hot_ready, 1)

                    def body(g):
                        dve.wait_ge(transposed, g.index + 1)
                        if g.back(2):
                            dve.wait_ge(roots_ready, g.index - 1)
                            dve.wait_ge(side_stored[g.pair], g.pair_round * 32)
                        v.tensor_copy(feat[g.pair][:, 0:g.width], item_t[g.pair][:, 0:g.width]).then_inc(feat_ready, 1)
                        if not g.late and g.back(HFIRST):
                            one_hots(g.back(HFIRST))
                        if g.late:
                            m = Group(g.i, g.j - SPLIT * SLOTS)
                            if not (g.static and g.index == GROUPS - 1):
                                pick_columns(dve, m)
                                hot_rows(dve, m.on(1))
                        dve.wait_ge(bars_loaded[g.slot], (g.round + 1) * 16)
                        dve.wait_ge(messages_ready, g.index + 1)
                        if g.back(1):
                            dve.wait_ge(scanned, g.index)
                        if g.back(2):
                            dve.wait_ge(rows_back, g.index - 1)
                        running_maximum(g, scan, messages).then_inc(scanned, 1)

                    def finish_counts():
                        dve.wait_ge(hot_used, HT // HSTEPS)
                        chain(v.tensor_copy(counts[:, :, :], hist[:, :].rearrange("p (g u) -> p g u", u=U)))
                        v.tensor_reduce(row_sum[:, :], counts[:, :, :], AX.X, ALU.add).then_inc(row_sums, 1)
                        v.tensor_scalar(filled[:, :, :], counts[:, :, :], 0.0, None, ALU.is_gt)
                        dve.wait_ge(src_all_loaded, 32)
                        v.tensor_scalar(part_a[:, :], src_all[:, :], 10, 2, ALU.logical_shift_right,
                                        ALU.logical_shift_left)
                        chain(v.tensor_scalar(part_b[:, :], src_all[:, :], U - 1, None, ALU.bitwise_and))
                        chain(v.tensor_tensor(src_col[:, :], part_a[:, :], part_b[:, :], ALU.add))
                        dve.wait_ge(sums_ready, 1)
                        two = rows_t[:, :, :].rearrange("p u d -> p (u d)")
                        chain(v.tensor_copy(total[:, :], two[:, GROUPS:2 * GROUPS]))
                        chain(v.tensor_tensor_scan(running[:, :], total[:, :], zeros[:, :], 0.0, ALU.add, ALU.add))
                        chain(v.tensor_tensor(base[:, :], running[:, :], total[:, :], ALU.subtract))
                        add = v.tensor_tensor(base[:, :], base[:, :], two[:, 0:GROUPS], ALU.add)
                        add.then_inc(sums_read, 1)
                        dve.wait_ge(sums_read, 1)
                        chain(v.tensor_tensor(cum[:, :, 0], counts[:, :, 0], base[:, :], ALU.add))
                        for u in range(1, U):
                            chain(v.tensor_tensor(cum[:, :, u], cum[:, :, u - 1], counts[:, :, u], ALU.add))
                        chain(v.tensor_scalar(cum[:, :, :], cum[:, :, :], none1[:, 0:1], None, ALU.subtract))
                        chain(v.tensor_tensor(cum[:, :, :], cum[:, :, :], filled[:, :, :], ALU.mult))
                        chain(v.tensor_scalar(cum[:, :, :], cum[:, :, :], none[:, 0:1], None, ALU.add))
                        chain(v.tensor_copy(node_last[:, 0:COLS].rearrange("p (g u) -> p g u", u=U), cum[:, :, :]))
                        v.tensor_scalar(part_a[:, :], node_last[:, 0:COLS], 8, 8, ALU.logical_shift_right,
                                        ALU.logical_shift_left)
                        chain(v.tensor_scalar(part_b[:, :], node_last[:, 0:COLS], 255, None, ALU.bitwise_and))
                        v.tensor_copy(high[:, :, :], part_a[:, :].rearrange("p (g u) -> p g u", u=U))
                        chain(v.tensor_copy(low[:, :, :], part_b[:, :].rearrange("p (g u) -> p g u", u=U)))
                        hot_rows(dve, Group(0, 0))

                    each_group(dve, body, between=finish_counts)

                @block.scalar
                def _(act):
                    s = nc.scalar
                    for to, what in ((w1[0:D, :], w1_msg), (w1[D:P, :], w1_edge), (root1[:, :], w1_root),
                                     (w2[0:D, :], w2_msg), (w2[D:P, :], w2_edge), (root2[0:D, :], w2_root)):
                        act.dma_start(to, what[:, :]).then_inc(weights_loaded, 16)
                    act.dma_start(bias1[:, :], b1.rearrange("(d o) -> d o", o=1)).then_inc(weights_loaded, 16)
                    act.dma_start(root2[D:D + 1, :], b2.rearrange("(o d) -> o d", o=1)).then_inc(weights_loaded, 16)
                    act.wait_ge(bar_ready, 1)
                    act.dma_start(barred.rearrange("(p t) -> p t", t=HT), bar[:, :]).then_inc(bar_stored, 16)
                    act.wait_ge(code_ready, 1)
                    act.dma_start(src_rows[0:EDGES].rearrange("(p t) -> p t", t=HT), src_code[:, :])\
                        .then_inc(code_stored, 16)
                    act.dma_start(src_rows[EDGES:GROUPS * GROUP].rearrange("(p t) -> p t", p=16),
                                  src_code[0:16, 0:(GROUPS * GROUP - EDGES) // 16]).then_inc(code_stored, 16)
                    act.wait_ge(weights_loaded, 16 * 8)

                    def sides(g):
                        act.wait_ge(roots_ready, g.index + 1)
                        if g.back(2):
                            act.wait_ge(side_stored[g.pair], g.pair_round * 32)
                        s.activation(side[g.pair][:, 0:g.width], roots[:, 0:g.width], ACT.Identity,
                                     bias=bias1[:, :]).then_inc(side_ready, 1)

                    def row_copy(g):
                        act.wait_ge(rows_back, g.index + 1)
                        if g.back(2):
                            act.wait_ge(rows_stored[g.pair], g.pair_round * 16)
                        s.activation(rows[g.pair][0:g.parts, :, 0:D], rows_t[0:g.parts, :, :], ACT.Copy)\
                            .then_inc(rows_ready, 1)

                    def store_rows(g):
                        act.wait_ge(rows_ready, g.index + 1)
                        act.dma_start(group_rows(maxima, g), rows[g.pair][0:g.parts, :, :])\
                            .then_inc(rows_stored[g.pair], 16)

                    def store_side(g):
                        act.dma_start(side_of(g, D, P), feat[g.pair][D:P, 0:g.width])\
                            .then_inc(side_stored[g.pair], 16)
                        act.wait_ge(side_ready, g.index + 1)
                        act.dma_start(side_of(g, 0, D), side[g.pair][:, 0:g.width])\
                            .then_inc(side_stored[g.pair], 16)

                    def body(g):
                        if g.back(1):
                            row_copy(g.back(1))
                            if g.static and g.index == 1:
                                act.wait_ge(halves_cleared, 2)
                            store_rows(g.back(1))
                        sides(g)
                        store_side(g)

                    each_group(act, body)
                    row_copy(Group(0, GROUPS - 1))
                    store_rows(Group(0, GROUPS - 1))

            with ExitStack() as phase:
                sb, ps, sem = make(phase)
                index = [sb(f"index_b{n}", [P, U], i32) for n in range(SLOTS)]
                item = [sb(f"item_b{n}", [P, U, D]) for n in range(SLOTS)]
                feat = [sb(f"feat_b{n}", [P, GROUP]) for n in range(SLOTS)]
                scan = [sb(f"scan_b{n}", [D, GROUP]) for n in range(2)]
                rows = [sb(f"rows_b{n}", [P, U, D]) for n in range(2)]
                item_t = [ps(f"item_tb{n}", [D, GROUP]) for n in range(2)]
                messages = ps("messages_b", [D, GROUP])
                rows_t = ps("rows_tb", [P, U, D])
                index_ready = sem("index_ready")
                side_loaded = [sem(f"side_loaded{n}") for n in range(SLOTS)]
                gathered = [sem(f"gathered_b{n}") for n in range(SLOTS)]
                transposed, summed, feat_ready = sem("transposed_b"), sem("summed"), sem("feat_ready_b")
                messages_ready, scanned = sem("messages_ready_b"), sem("scanned_b")
                rows_back, rows_ready = sem("rows_back_b"), sem("rows_ready_b")
                rows_stored = [sem(f"rows_stored_b{n}") for n in range(2)]
                pool_step = sem("pool_step_b")
                block = phase.enter_context(nc.Block())

                @block.sync
                def _(sp):
                    def body(g):
                        if g.back(SLOTS):
                            sp.wait_ge(messages_ready, g.index - SLOTS + 1)
                        sp.dma_start(feat[g.slot][:, 0:g.width], side_of(g, 0, P))\
                            .then_inc(side_loaded[g.slot], 16)
                        if not g.late:
                            load_src_row(sp, Group(g.i, g.j + LOOKED1))

                    for j in range(SLOTS):
                        load_node_index(sp, Group(0, j))
                    each_group(sp, body)
                    for n in range(2):
                        sp.wait_ge(rows_stored[n], 16 * (GROUPS // 2))

                @block.gpsimd
                def _(pool):
                    def body(g):
                        pool.wait_ge(index_ready, g.index + 1)
                        if g.back(SLOTS):
                            pool.wait_ge(transposed, g.index - SLOTS + 1)
                        pool.sem_inc(pool_step, 1)
                        for u in range(U):
                            nc.gpsimd.indirect_dma_start(
                                item[g.slot][0:g.parts, u, :], None, maxima_halves[:, :],
                                bass.IndirectOffsetOnAxis(ap=index[g.slot][0:g.parts, u:u + 1], axis=0),
                            ).then_inc(gathered[g.slot], 16)

                    each_group(pool, body)

                @block.tensor
                def _(pe):
                    def arrive(g):
                        pe.wait_ge(gathered[g.slot], (g.round + 1) * 64)
                        if g.back(2):
                            pe.wait_ge(summed, g.index - 1)
                        for u in range(U):
                            last = nc.tensor.transpose(item_t[g.pair][:, u:g.width:U], item[g.slot][0:g.parts, u, :],
                                                       ident[0:g.parts, 0:g.parts])
                        last.then_inc(transposed, 1)

                    def products(g):
                        pe.wait_ge(feat_ready, g.index + 1)
                        if g.back(1):
                            pe.wait_ge(scanned, g.index)
                        nc.tensor.matmul(messages[:, 0:g.width], w2[:, :], feat[g.slot][:, 0:g.width],
                                         start=True, stop=True).then_inc(messages_ready, 1)

                    def go_back(g):
                        pe.wait_ge(scanned, g.index + 1)
                        if g.back(1):
                            pe.wait_ge(rows_ready, g.index)
                        for u in range(U):
                            last = nc.tensor.transpose(rows_t[0:g.parts, u, :], scan[g.pair][:, u:g.width:U],
                                                       ident[0:D, 0:D])
                        last.then_inc(rows_back, 1)

                    def body(g):
                        arrive(g)
                        if not g.late:
                            pick_rows(pe, Group(g.i, g.j + LOOKED1 - 1))
                        if g.back(1):
                            go_back(g.back(1))
                        products(g)

                    each_group(pe, body, between=lambda: pick_rows(pe, Group(0, GROUPS - 1)))
                    go_back(Group(0, GROUPS - 1))

                @block.vector
                def _(dve):
                    v = nc.vector

                    def take_index(g):
                        if g.back(SLOTS):
                            dve.wait_ge(gathered[g.slot], g.round * 64)
                        v.tensor_scalar(index[g.slot][0:g.parts, :], src_last[0:g.parts, bass.ds(g.index * U, U)],
                                        2.0, None, ALU.mult).then_inc(index_ready, 1)

                    def body(g):
                        if g.on(3):
                            take_index(g.on(3))
                        dve.wait_ge(transposed, g.index + 1)
                        dve.wait_ge(side_loaded[g.slot], (g.round + 1) * 16)
                        v.tensor_tensor(feat[g.slot][0:D, 0:g.width], item_t[g.pair][:, 0:g.width],
                                        feat[g.slot][0:D, 0:g.width], ALU.add).then_inc(summed, 1)
                        dve.wait_ge(summed, g.index + 1)
                        v.scalar_tensor_tensor(out=feat[g.slot][0:D, 0:g.width], in0=feat[g.slot][0:D, 0:g.width],
                                               scalar=SLOPE, in1=feat[g.slot][0:D, 0:g.width],
                                               op0=ALU.mult, op1=ALU.max).then_inc(feat_ready, 1)
                        if not g.late:
                            pick_columns(dve, Group(g.i, g.j + LOOKED1 - 1))
                            hot_rows(dve, Group(g.i, g.j + LOOKED1))
                        dve.wait_ge(messages_ready, g.index + 1)
                        if g.back(1):
                            dve.wait_ge(scanned, g.index)
                        if g.back(2):
                            dve.wait_ge(rows_back, g.index - 1)
                        running_maximum(g, scan, messages).then_inc(scanned, 1)

                    dve.wait_ge(looked_up, LOOKED1 - 1)
                    for j in range(3):
                        take_index(Group(0, j))
                    each_group(dve, body, between=lambda: pick_columns(dve, Group(0, GROUPS - 1)))

                @block.scalar
                def _(act):
                    s = nc.scalar

                    def body(g):
                        act.wait_ge(rows_back, g.index + 1)
                        if g.back(2):
                            act.wait_ge(rows_stored[g.pair], g.pair_round * 16)
                        s.activation(rows[g.pair][0:g.parts, :, :], rows_t[0:g.parts, :, :], ACT.Copy)\
                            .then_inc(rows_ready, 1)
                        act.wait_ge(rows_ready, g.index + 1)
                        act.dma_start(group_rows(maxima[:, D:2 * D], g), rows[g.pair][0:g.parts, :, :])\
                            .then_inc(rows_stored[g.pair], 16)

                    each_group(act, body)

        with ExitStack() as phase:
            sb, ps, sem = make(phase)
            item = [sb(f"item_n{n}", [P, U, 2 * D]) for n in range(SLOTS)]
            xs = [sb(f"xs{n}", [P, U, D]) for n in range(SLOTS)]
            x_cols = [sb(f"x_cols{n}", [D, GROUP]) for n in range(2)]
            c1 = [sb(f"c1_{n}", [D + 1, GROUP]) for n in range(2)]
            biased = [sb(f"biased{n}", [D, GROUP]) for n in range(2)]
            c2 = [sb(f"c2_{n}", [P, U, D]) for n in range(2)]
            y = [sb(f"y{n}", [P, U, D]) for n in range(4)]
            result = [sb(f"result{n}", [P, U, D]) for n in range(2)]
            stats = [sb(f"stats{n}", [P, U, 6]) for n in range(2)]
            mean_var = [sb(f"mean_var{n}", [P, U, 2]) for n in range(2)]
            std = [sb(f"std{n}", [P, U]) for n in range(2)]
            rstd = [sb(f"rstd{n}", [P, U]) for n in range(4)]
            shift = [sb(f"shift{n}", [P, U]) for n in range(4)]
            eps = sb("eps", [P, 1])
            x_t = [ps(f"x_t{n}", [D, GROUP]) for n in range(2)]
            pre1 = [ps(f"pre1_{n}", [D, GROUP]) for n in range(2)]
            pre2 = [ps(f"pre2_{n}", [P, U, D]) for n in range(2)]
            x_loaded = [sem(f"x_loaded_n{n}") for n in range(SLOTS)]
            gathered = [sem(f"gathered_n{n}") for n in range(SLOTS)]
            const_ready, x_transposed, x_ready = sem("const_ready"), sem("x_transposed"), sem("x_ready")
            pre1_ready, c1_ready = sem("pre1_ready"), sem("c1_ready")
            biased_ready, scaled_ready = sem("biased_ready"), sem("scaled_ready")
            pre2_ready, c2_ready = sem("pre2_ready"), sem("c2_ready")
            y_ready, stats_ready, var_ready = sem("y_ready"), sem("stats_ready"), sem("var_ready")
            std_ready, rstd_ready, result_ready = sem("std_ready"), sem("rstd_ready"), sem("result_ready")
            shift_ready = sem("shift_ready")
            result_stored = [sem(f"result_stored{n}") for n in range(2)]
            pool_step, dve_step = sem("pool_step_n"), sem("dve_step")
            block = phase.enter_context(nc.Block())

            @block.sync
            def _(sp):
                def body(g):
                    new = g.on(1)
                    if new and new.back(SLOTS):
                        sp.wait_ge(gathered[new.slot], new.round * 64)
                        load_node_index(sp, new)
                    if g.back(SLOTS):
                        sp.wait_ge(y_ready, g.index - SLOTS + 1)
                    sp.dma_start(xs[g.slot][0:g.parts, :, :], group_rows(x, g)).then_inc(x_loaded[g.slot], 16)

                each_group(sp, body)
                for n in range(2):
                    sp.wait_ge(result_stored[n], 16 * (GROUPS // 2))

            @block.gpsimd
            def _(pool):
                def body(g):
                    pool.wait_ge(node_index_loaded[g.slot], (g.round + 1) * 16)
                    if g.back(SLOTS):
                        pool.wait_ge(pre2_ready, g.index - SLOTS + 1)
                    pool.sem_inc(pool_step, 1)
                    for u in range(U):
                        nc.gpsimd.indirect_dma_start(
                            item[g.slot][0:g.parts, u, :], None, maxima[:, :],
                            bass.IndirectOffsetOnAxis(ap=node_index[g.slot][0:g.parts, u:u + 1], axis=0),
                        ).then_inc(gathered[g.slot], 16)

                each_group(pool, body)

            @block.tensor
            def _(pe):
                def x_columns(g):
                    pe.wait_ge(x_loaded[g.slot], (g.round + 1) * 16)
                    if g.back(2):
                        pe.wait_ge(x_ready, g.index - 1)
                    for u in range(U):
                        last = nc.tensor.transpose(x_t[g.pair][:, u:g.width:U], xs[g.slot][0:g.parts, u, :],
                                                   ident[0:g.parts, 0:g.parts])
                    last.then_inc(x_transposed, 1)

                def layer1(g):
                    pe.wait_ge(x_ready, g.index + 1)
                    if g.back(2):
                        pe.wait_ge(biased_ready, g.index - 1)
                    nc.tensor.matmul(pre1[g.pair][:, 0:g.width], root1[:, :], x_cols[g.pair][:, 0:g.width],
                                     start=True, stop=False)
                    pe.wait_ge(gathered[g.slot], (g.round + 1) * 64)
                    for u in range(U):
                        last = nc.tensor.matmul(pre1[g.pair][:, u:g.width:U], item[g.slot][0:g.parts, u, 0:D],
                                                ident[0:g.parts, 0:g.parts], start=False, stop=(u == U - 1))
                    last.then_inc(pre1_ready, 1)

                def layer2(g):
                    pe.wait_ge(c1_ready, g.index + 1)
                    if g.back(2):
                        pe.wait_ge(c2_ready, g.index - 1)
                    nc.tensor.matmul(pre2[g.pair][0:g.parts, :, :], ident[0:g.parts, 0:g.parts],
                                     item[g.slot][0:g.parts, :, D:2 * D], start=True, stop=False)
                    for u in range(U):
                        last = nc.tensor.matmul(pre2[g.pair][0:g.parts, u, :], c1[g.pair][:, u:g.width:U],
                                                root2[:, :], start=False, stop=(u == U - 1))
                    last.then_inc(pre2_ready, 1)

                def body(g):
                    if g.on(1):
                        x_columns(g.on(1))
                    layer1(g)
                    if g.back(1):
                        layer2(g.back(1))

                x_columns(Group(0, 0))
                each_group(pe, body)
                layer2(Group(0, GROUPS - 1))

            @block.vector
            def _(dve):
                v = nc.vector

                def leak1(g):
                    dve.wait_ge(biased_ready, g.index + 1)
                    if g.back(2):
                        dve.wait_ge(pre2_ready, g.index - 1)
                    v.scalar_tensor_tensor(out=c1[g.pair][0:D, 0:g.width], in0=biased[g.pair][:, 0:g.width],
                                           scalar=SLOPE, in1=biased[g.pair][:, 0:g.width],
                                           op0=ALU.mult, op1=ALU.max).then_inc(c1_ready, 1)

                def lower(g):
                    dve.wait_ge(scaled_ready, g.index + 1)
                    v.scalar_tensor_tensor(out=c2[g.pair][0:g.parts, :, :], in0=pre2[g.pair][0:g.parts, :, :],
                                           scalar=1.0, in1=c2[g.pair][0:g.parts, :, :],
                                           op0=ALU.mult, op1=ALU.max).then_inc(c2_ready, 1)

                def add_x(g):
                    dve.wait_ge(c2_ready, g.index + 1)
                    if g.back(4):
                        dve.wait_ge(result_ready, g.index - 3)
                    v.tensor_tensor(y[g.quad][0:g.parts, :, :], c2[g.pair][0:g.parts, :, :],
                                    xs[g.slot][0:g.parts, :, :], ALU.add).then_inc(y_ready, 1)

                def take_stats(g):
                    dve.wait_ge(y_ready, g.index + 1)
                    for u in range(U):
                        last = v.bn_stats(stats[g.pair][0:g.parts, u, :], y[g.quad][0:g.parts, u, :])
                    last.then_inc(stats_ready, 1)

                def moments(g):
                    dve.wait_ge(stats_ready, g.index + 1)
                    dve.sem_inc(dve_step, 1)
                    for u in range(U):
                        last = v.bn_aggr(mean_var[g.pair][0:g.parts, u, :], stats[g.pair][0:g.parts, u, :])
                    last.then_inc(var_ready, 1)

                def invert(g):
                    dve.wait_ge(std_ready, g.index + 1)
                    if g.back(4):
                        dve.wait_ge(result_ready, g.index - 3)
                    v.reciprocal(rstd[g.quad][0:g.parts, :], std[g.pair][0:g.parts, :]).then_inc(rstd_ready, 1)

                def find_shift(g):
                    dve.wait_ge(rstd_ready, g.index + 1)
                    if g.back(4):
                        dve.wait_ge(result_ready, g.index - 3)
                    v.scalar_tensor_tensor(out=shift[g.quad][0:g.parts, :], in0=mean_var[g.pair][0:g.parts, :, 0],
                                           scalar=-1.0, in1=rstd[g.quad][0:g.parts, :],
                                           op0=ALU.mult, op1=ALU.mult).then_inc(shift_ready, 1)

                def step(new, middle, old):
                    if middle:
                        lower(middle)
                    if old:
                        invert(old)
                    if middle:
                        add_x(middle)
                    if old:
                        find_shift(old)
                    if middle:
                        take_stats(middle)
                    if new:
                        leak1(new)
                    if middle:
                        moments(middle)

                def body(g):
                    step(g, g.back(2), g.back(3))

                v.memset(eps[:, :], EPS).then_inc(const_ready, 1)
                for n in range(2):
                    v.memset(c1[n][D:D + 1, :], 1.0).then_inc(const_ready, 1)
                each_group(dve, body)
                before_last, last = Group(0, GROUPS - 2), Group(0, GROUPS - 1)
                step(None, before_last, Group(0, GROUPS - 3))
                lower(last)
                add_x(last)
                take_stats(last)
                invert(before_last)
                moments(last)
                find_shift(before_last)
                invert(last)
                find_shift(last)

            @block.scalar
            def _(act):
                s = nc.scalar

                def x_copy(g):
                    act.wait_ge(x_transposed, g.index + 1)
                    if g.back(2):
                        act.wait_ge(pre1_ready, g.index - 1)
                    s.activation(x_cols[g.pair][:, 0:g.width], x_t[g.pair][:, 0:g.width], ACT.Copy)\
                        .then_inc(x_ready, 1)

                def bias(g):
                    act.wait_ge(pre1_ready, g.index + 1)
                    if g.back(2):
                        act.wait_ge(c1_ready, g.index - 1)
                    s.activation(biased[g.pair][:, 0:g.width], pre1[g.pair][:, 0:g.width], ACT.Identity,
                                 bias=bias1[:, :]).then_inc(biased_ready, 1)

                def scale(g):
                    act.wait_ge(pre2_ready, g.index + 1)
                    if g.back(2):
                        act.wait_ge(y_ready, g.index - 1)
                    s.activation(c2[g.pair][0:g.parts, :, :], pre2[g.pair][0:g.parts, :, :], ACT.Copy,
                                 scale=SLOPE).then_inc(scaled_ready, 1)

                def root(g):
                    act.wait_ge(var_ready, g.index + 1)
                    if g.back(2):
                        act.wait_ge(rstd_ready, g.index - 1)
                    s.activation(std[g.pair][0:g.parts, :], mean_var[g.pair][0:g.parts, :, 1], ACT.Sqrt,
                                 bias=eps[0:g.parts, :]).then_inc(std_ready, 1)

                def normalize(g):
                    act.wait_ge(shift_ready, g.index + 1)
                    if g.back(2):
                        act.wait_ge(result_stored[g.pair], g.pair_round * 16)
                    for u in range(U):
                        last = s.activation(result[g.pair][0:g.parts, u, :], y[g.quad][0:g.parts, u, :], ACT.Identity,
                                            scale=rstd[g.quad][0:g.parts, u:u + 1],
                                            bias=shift[g.quad][0:g.parts, u:u + 1])
                    last.then_inc(result_ready, 1)

                def store(g):
                    act.wait_ge(result_ready, g.index + 1)
                    act.dma_start(group_rows(out, g), result[g.pair][0:g.parts, :, :])\
                        .then_inc(result_stored[g.pair], 16)

                def body(g):
                    if g.back(3):
                        root(g.back(3))
                    if g.on(1):
                        x_copy(g.on(1))
                    bias(g)
                    if g.back(1):
                        scale(g.back(1))
                    if g.back(4):
                        normalize(g.back(4))
                        store(g.back(4))

                act.wait_ge(const_ready, 3)
                x_copy(Group(0, 0))
                each_group(act, body)
                root(Group(0, GROUPS - 3))
                scale(Group(0, GROUPS - 1))
                normalize(Group(0, GROUPS - 4))
                store(Group(0, GROUPS - 4))
                root(Group(0, GROUPS - 2))
                normalize(Group(0, GROUPS - 3))
                store(Group(0, GROUPS - 3))
                root(Group(0, GROUPS - 1))
                normalize(Group(0, GROUPS - 2))
                store(Group(0, GROUPS - 2))
                normalize(Group(0, GROUPS - 1))
                store(Group(0, GROUPS - 1))


_INS = ["x", "src", "dst", "edge_attr_32", "L0_gnn_W1_msg", "L0_gnn_W1_edge", "L0_gnn_W1_root", "L0_gnn_b1",
        "L0_gnn_W2_msg", "L0_gnn_W2_edge", "L0_gnn_W2_root", "L0_gnn_b2"]


def kernel(**inputs):
    import numpy as _np
    import concourse.bacc as _bacc
    from concourse import mybir as _mybir
    from concourse.bass_utils import run_bass_kernel_spmd as _run

    nc = _bacc.Bacc("TRN2", target_bir_lowering=False, num_devices=1)
    arrays, args = {}, []
    for name in _INS:
        a = _np.ascontiguousarray(inputs[name])
        arrays[f"in_{name}"] = a
        args.append(nc.dram_tensor(f"in_{name}", a.shape, _mybir.dt.from_np(a.dtype), kind="ExternalInput").ap())
    args.append(nc.dram_tensor("out_0", (NODES, D), _mybir.dt.float32, kind="ExternalOutput").ap())
    build_gnn(nc, *args)
    return _run(nc, [arrays], core_ids=[0]).results[0]["out_0"]
```
